# Optimizing a Trainium2 kernel written in Bass

```python
import numpy as np
import jax
import jax.numpy as jnp

def _softmax(x, axis=-1):
    return jax.nn.softmax(x, axis=axis)

def _gelu(x):
    return jax.nn.gelu(x, approximate=True)

def _silu(x):
    return jax.nn.silu(x)

def _sigmoid(x):
    return jax.nn.sigmoid(x)

def _layernorm(x, axis=-1, eps=1e-05):
    m = jnp.mean(x, axis=axis, keepdims=True)
    v = jnp.var(x, axis=axis, keepdims=True)
    return (x - m) / jnp.sqrt(v + eps)

def _scatter_add(tgt, idx, src, axis=0):
    return tgt.at[idx].add(src)

def _segment_sum(src, seg, n):
    return jax.ops.segment_sum(src, seg, n)
kernel_name = 'mk_rec_standalone_d1_rec_r8_6adf0b'

def setup_inputs(seed: int=0):
    np.random.seed(seed)
    _w = jnp.asarray

    def _rec_inputs():
        import jax
        import jax.numpy as jnp
        _rk = jax.random.key(seed)
        r_x = -0.000611745 + 1.00059 * jax.random.normal(jax.random.fold_in(_rk, 1), (512, 39, 64), jnp.float32)
        return r_x
    r_x = _rec_inputs()

    def _L0_rec_setup():
        import jax, jax.numpy as jnp
        import numpy as np
        B, M, D = (1024, 39, 64)
        H1, H2 = (128, 128)

        def _cin_forward(x, Ws):
            x0 = x
            h = x
            outs = []
            for W in Ws:
                h = jnp.einsum('bid,bjd,ijh->bhd', x0, h, W)
                outs.append(h)
            out = jnp.concatenate(outs, axis=1)
            return out.sum(axis=-1)
        key = jax.random.key(seed)
        kx, k0, k1 = jax.random.split(key, 3)
        x = jax.random.normal(kx, (B, M, D), dtype=jnp.float32)
        W0 = jax.random.uniform(k0, (M, M, H1), minval=-0.05, maxval=0.05, dtype=jnp.float32)
        W1 = jax.random.uniform(k1, (M, H1, H2), minval=-0.05, maxval=0.05, dtype=jnp.float32)
        return {'x': x, 'W0': W0, 'W1': W1}
    _L0_rec_all = _L0_rec_setup()
    _L0_rec_in = {k: v for k, v in _L0_rec_all.items() if k in ('W0', 'W1')}
    del _L0_rec_all
    return {'r_x': r_x, 'L0_rec_W0': _L0_rec_in['W0'], 'L0_rec_W1': _L0_rec_in['W1']}

def reference(r_x, L0_rec_W0, L0_rec_W1):
    import jax
    import jax.numpy as jnp

    def _L0_rec_ref(x, W0, W1):
        import jax, jax.numpy as jnp
        import numpy as np
        B, M, D = (1024, 39, 64)
        H1, H2 = (128, 128)

        def _cin_forward(x, Ws):
            x0 = x
            h = x
            outs = []
            for W in Ws:
                h = jnp.einsum('bid,bjd,ijh->bhd', x0, h, W)
                outs.append(h)
            out = jnp.concatenate(outs, axis=1)
            return out.sum(axis=-1)
        return _cin_forward(x, (W0, W1))
    y = _L0_rec_ref(r_x, L0_rec_W0, L0_rec_W1)
    return y

_drawn_inputs = setup_inputs


def setup_inputs(seed=0):
    import zlib

    import numpy as np

    out = dict(_drawn_inputs(seed))
    spreads = {}
    factors = {}
    for name, (base, spread) in spreads.items():
        noise = np.random.default_rng([zlib.crc32(name.encode()), seed]).standard_normal(out[name].shape)
        drawn = base * np.exp(spread * noise) if base else spread * noise
        out[name] = jnp.asarray(drawn.astype(out[name].dtype))
    for name, factor in factors.items():
        out[name] = (out[name] * factor).astype(out[name].dtype)
    return out
```

```python
from contextlib import ExitStack

import concourse.bass as bass
from concourse import mybir

F32 = mybir.dt.float32
F32R = mybir.dt.float32r
ALU = mybir.AluOpType

PRODUCTS = [(0, 1), (1, 2), (2, 0), (0, 3), (1, 4), (3, 4)]
OFFSETS = [[19, 31, 27, 22, 15], [14, 28, 19, 15, 9], [29, 12, 14, 1, 30]]
EXTRA_START = [0, 13, 26, 0, 13]
SMALL_RUNS = [(11, 24, 2), (24, 37, 2), (37, 11, 2), (11, 11, 2), (23, 23, 16)]
FULL = [0, 1, 2]
SPLIT = [3, 4, 5]


def covered_pairs(fields, extra):
    seen, rows = set(), []
    for t, (r, s) in enumerate(PRODUCTS):
        for g, offset in enumerate(OFFSETS):
            for k in range(fields):
                rows.append((t, g * fields + k, (k + offset[r]) % fields, (k + offset[s]) % fields))
        for m in range(extra if t < 5 else 0):
            rows.append((t, 3 * fields + m, EXTRA_START[r] + m, EXTRA_START[s] + m))
    at = 0
    for left, right, n in SMALL_RUNS:
        for m in range(n):
            if (left + m, right + m) != (23, 23):
                rows.append((6, at + m, left + m, right + m))
        at += n
    for row in rows:
        pair = frozenset(row[2:])
        assert pair not in seen
        seen.add(pair)
    assert len(seen) == fields * (fields + 1) // 2
    return rows


def cin_kernel(nc: bass.Bass, x: bass.AP, w0: bass.AP, w1: bass.AP, out: bass.AP):
    BATCH, FIELDS, DIM = x.shape
    HID = w0.shape[2]
    P = 128
    COLS = BATCH * DIM
    STEP = 1024
    STEP_B = STEP // DIM
    STEPS = COLS // STEP
    BANK = 512
    SUBS = STEP // BANK
    PAIRS_B = STEP_B // 2
    PER_BANK = PAIRS_B // 2
    ROUND = P // STEP_B
    ROUNDS = STEPS // ROUND
    NT = 5
    EXTRA = P - 3 * FIELDS
    SMALL = sum(n for _, _, n in SMALL_RUNS)
    NS = len(SPLIT)
    TILES = len(FULL) + NS + 1
    GW = 48
    ONES = FIELDS
    PIECE_B = 64
    PIECES = BATCH // PIECE_B
    STEPS_A_PIECE = PIECE_B // STEP_B
    QUAD = 32
    covered_pairs(FIELDS, EXTRA)

    x_rows = nc.dram_tensor("x_rows", (2 * FIELDS, COLS), F32).ap()
    small_rows = nc.dram_tensor("small_rows", (2, SMALL, COLS), F32).ap()
    w_sum = nc.dram_tensor("w_sum", (2 * FIELDS, 2 * FIELDS, HID), F32).ap()
    w_sum_rows = w_sum.rearrange("u v h -> (u v) h")
    w0_rows = w0.rearrange("u v h -> (u v) h")

    ctx = ExitStack()
    with ctx:
        def sb(name, shape, dt=F32):
            return ctx.enter_context(nc.sbuf_tensor(name, shape, dt))

        def sem(name):
            return ctx.enter_context(nc.semaphore(name))

        operands = sb("operands", [P, 2, NT, STEP])
        small_operands = sb("small_operands", [QUAD, 2, 2, STEP])
        full_prod = sb("full_prod", [P, len(FULL), STEP])
        split_prod = sb("split_prod", [P, 2, STEP])
        split_hi = sb("split_hi", [P, NS, STEP], F32R)
        split_lo = sb("split_lo", [P, NS, STEP], F32R)
        small_prod = sb("small_prod", [QUAD, STEP])
        small_parts = sb("small_parts", [P, STEP], F32R)
        h1 = sb("h1", [P, STEP])
        h1_t = sb("h1_t", [P, PAIRS_B, HID])
        x_nat = sb("x_nat", [2 * FIELDS, 2, PAIRS_B, DIM])
        x_diag = sb("x_diag", [P, PAIRS_B, 2 * GW])
        gram = sb("gram", [P, FIELDS + 1, P])
        w1_sb = sb("w1_sb", [P, FIELDS, HID])
        w_full = sb("w_full", [P, len(PRODUCTS), HID])
        w_hi = sb("w_hi", [P, NS, HID], F32R)
        w_lo = sb("w_lo", [P, NS, HID], F32R)
        w_small = sb("w_small", [QUAD, HID])
        w_small_parts = sb("w_small_parts", [P, HID], F32R)
        w_straight = sb("w_straight", [FIELDS, FIELDS * HID])
        w_turned = gram[0:FIELDS, 0:FIELDS, :]
        ident = sb("ident", [P, P])
        out_sb = sb("out_sb", [P, 2 * HID])

        def bank(name):
            return ctx.enter_context(nc.psum_tensor(name, [P, BANK], F32))

        acc = [[bank(f"acc{p}{s}") for s in range(SUBS)] for p in range(2)]
        h1_t_ps = bank("h1_t_ps")
        x_t_ps = bank("x_t_ps")
        gram_ps = [bank("gram_ps0"), bank("gram_ps1")]

        rows_ready = [sem("rows_ready_even"), sem("rows_ready_odd")]
        small_rows_ready = sem("small_rows_ready")
        w0_loaded = sem("w0_loaded")
        w_summed = sem("w_summed")
        w_sum_stored = sem("w_sum_stored")
        w_loaded = sem("w_loaded")
        w1_loaded = sem("w1_loaded")
        zeroed = sem("zeroed")
        pool_zeroed = sem("pool_zeroed")
        constants_ready = sem("constants_ready")
        w_hi_ready = sem("w_hi_ready")
        w_parts_ready = sem("w_parts_ready")
        w_small_lo_ready = sem("w_small_lo_ready")
        operands_loaded = [sem("operands_loaded0"), sem("operands_loaded1")]
        x_nat_loaded = [sem("x_nat_loaded0"), sem("x_nat_loaded1")]
        full_ready = sem("full_ready")
        split_ready = sem("split_ready")
        hi_ready = sem("hi_ready")
        lo_ready = sem("lo_ready")
        small_ready = sem("small_ready")
        small_hi_ready = sem("small_hi_ready")
        small_lo_ready = sem("small_lo_ready")
        small_parts_ready = sem("small_parts_ready")
        tile_done = sem("tile_done")
        h1_ready = sem("h1_ready")
        x_transposed = sem("x_transposed")
        x_diag_ready = sem("x_diag_ready")
        h1_transposed = sem("h1_transposed")
        h1_t_ready = sem("h1_t_ready")
        gram_done = sem("gram_done")
        gram_ready = sem("gram_ready")
        round_done = sem("round_done")
        round_copied = sem("round_copied")
        out_stored = sem("out_stored")

        ORDER = [("full", 0), ("full", 1), ("split", 0), ("full", 2), ("split", 1), ("split", 2), ("small", 0)]
        PLACE = {what: n for n, what in enumerate(ORDER)}

        def tiles_through(n, what):
            return n * TILES + PLACE[what] + 1

        OPERAND_DMAS = 4 * NT + 2
        HALF_X = 2
        W_LOADS = 16 * (3 * len(PRODUCTS) + 5 + len(SMALL_RUNS))

        block = ctx.enter_context(nc.Block())

        def run_steps(eng, step, last):
            step(0, 0)
            step(1, 1)
            with eng.Fori(0, ROUNDS - 1) as q:
                for s in range(2, ROUND + 2):
                    step(q * ROUND + s, s)
            for s in range(2, ROUND):
                step((ROUNDS - 1) * ROUND + s, s)
            last()

        @block.gpsimd
        def _(pool):
            def copy_piece(p):
                b0 = p * PIECE_B
                src = x[b0:b0 + PIECE_B]
                for copy in range(2):
                    dst = x_rows[copy * FIELDS:(copy + 1) * FIELDS, b0 * DIM:(b0 + PIECE_B) * DIM]
                    pool.dma_start(dst.rearrange("k (b d) -> b k d", d=DIM), src).then_inc(rows_ready[p % 2], 16)

            copy_piece(0)
            copy_piece(1)
            at = 0
            for left, right, n in SMALL_RUNS:
                for side, row in ((0, left), (1, right)):
                    dst = small_rows[side, at:at + n, :].rearrange("k (b d) -> b k d", d=DIM)
                    pool.dma_start(dst, x[:, row:row + n, :]).then_inc(small_rows_ready, 16)
                at += n

            nc.gpsimd.memset(small_operands[:, :, :, :], 0.0).then_inc(pool_zeroed, 1)
            nc.gpsimd.memset(x_diag[:, :, :], 0.0).then_inc(pool_zeroed, 1)
            nc.gpsimd.memset(ident[:, :], 0.0).then_inc(pool_zeroed, 1)
            pool.wait_ge(pool_zeroed, 3)
            nc.gpsimd.memset(x_diag[0:DIM, :, ONES:ONES + 1], 1.0).then_inc(constants_ready, 1)
            nc.gpsimd.memset(x_diag[DIM:P, :, GW + ONES:GW + ONES + 1], 1.0).then_inc(constants_ready, 1)
            pool.wait_ge(constants_ready, 2)
            nc.gpsimd.affine_select(out=ident[:, :], in_=ident[:, :], compare_op=ALU.not_equal, fill=1.0, base=0,
                                    pattern=[[-1, P]], channel_multiplier=1).then_inc(constants_ready, 1)
            for p in range(2, PIECES):
                pool.wait_ge(rows_ready[p % 2], 32 * (p // 2))
                copy_piece(p)

        @block.sync
        def _(sp):
            sp.dma_start(w_straight[:, :], w0.rearrange("u v h -> u (v h)")).then_inc(w0_loaded, 16)
            sp.dma_start(w_turned, w0.rearrange("u v h -> v u h")).then_inc(w0_loaded, 16)

            def load_x_nat(n, s):
                if s >= 2:
                    sp.wait_ge(x_transposed, n - 1)
                for half in range(2):
                    b0 = n * STEP_B + half * PAIRS_B
                    sp.dma_start(x_nat[half * FIELDS:(half + 1) * FIELDS, s % 2, :, :],
                                 x[bass.ds(b0, PAIRS_B)].rearrange("b i d -> i b d"))\
                        .then_inc(x_nat_loaded[s % 2], 16)

            def load_operands(n, s, round_):
                piece_in_round = (s % ROUND) // STEPS_A_PIECE
                sp.wait_ge(rows_ready[piece_in_round], round_ * 32 + 32)
                if s >= 2:
                    sp.wait_ge(small_ready, n - 1)
                c0 = n * STEP
                for r in range(NT):
                    for g in range(3):
                        a = OFFSETS[g][r]
                        sp.dma_start(operands[g * FIELDS:(g + 1) * FIELDS, s % 2, r, :],
                                     x_rows[a:a + FIELDS, bass.ds(c0, STEP)]).then_inc(operands_loaded[s % 2], 16)
                    a = EXTRA_START[r]
                    sp.dma_start(operands[3 * FIELDS:P, s % 2, r, :],
                                 x_rows[a:a + EXTRA, bass.ds(c0, STEP)]).then_inc(operands_loaded[s % 2], 16)
                for side in range(2):
                    sp.dma_start(small_operands[0:SMALL, s % 2, side, :],
                                 small_rows[side, :, bass.ds(c0, STEP)]).then_inc(operands_loaded[s % 2], 16)

            def load_weights():
                sp.wait_ge(w_summed, 1)
                for u in range(2):
                    for v in range(2):
                        sp.dma_start(w_sum[u * FIELDS:(u + 1) * FIELDS, v * FIELDS:(v + 1) * FIELDS, :],
                                     w_straight[:, :].rearrange("u (v h) -> u v h", h=HID)).then_inc(w_sum_stored, 16)
                sp.wait_ge(w_sum_stored, 64)
                sp.wait_ge(zeroed, 2)

                def rows(dst, left, right, n):
                    if left == right:
                        src = w0_rows[left * (FIELDS + 1):(left + n - 1) * (FIELDS + 1) + 1:FIELDS + 1, :]
                    else:
                        first = left * 2 * FIELDS + right
                        src = w_sum_rows[first:first + (n - 1) * (2 * FIELDS + 1) + 1:2 * FIELDS + 1, :]
                    sp.dma_start(dst, src).then_inc(w_loaded, 16)
                    return 16

                total = 0
                for t, (r, s) in enumerate(PRODUCTS):
                    for g, offset in enumerate(OFFSETS):
                        total += rows(w_full[g * FIELDS:(g + 1) * FIELDS, t, :], offset[r], offset[s], FIELDS)
                    if t < 5:
                        total += rows(w_full[3 * FIELDS:P, t, :], EXTRA_START[r], EXTRA_START[s], EXTRA)
                at = 0
                for left, right, n in SMALL_RUNS:
                    skip = int((left, right) == (23, 23))
                    total += rows(w_small[at + skip:at + n, :], left + skip, right + skip, n - skip)
                    at += n
                assert total == W_LOADS
                sp.dma_start(w1_sb[:, :, :], w1.rearrange("i j h -> j i h")).then_inc(w1_loaded, 16)

            load_x_nat(0, 0)
            load_x_nat(1, 1)
            load_weights()
            sp.wait_ge(small_rows_ready, 16 * 2 * len(SMALL_RUNS))
            sp.wait_ge(pool_zeroed, 3)
            load_operands(0, 0, 0)
            load_operands(1, 1, 0)
            with sp.Fori(0, ROUNDS - 1) as q:
                for s in range(2, ROUND + 2):
                    load_operands(q * ROUND + s, s, q + s // ROUND)
                    load_x_nat(q * ROUND + s, s)
            for s in range(2, ROUND):
                n = (ROUNDS - 1) * ROUND + s
                load_operands(n, s, ROUNDS - 1)
                load_x_nat(n, s)

        @block.vector
        def _(dve):
            nc.vector.memset(w_full[:, :, :], 0.0).then_inc(zeroed, 1)
            nc.vector.memset(w_small[:, :], 0.0).then_inc(zeroed, 1)
            dve.wait_ge(w0_loaded, 32)
            nc.vector.tensor_tensor(w_straight[:, :], w_straight[:, :], w_turned.rearrange("u v h -> u (v h)"),
                                    ALU.add).then_inc(w_summed, 1)
            dve.wait_ge(w_hi_ready, 3)
            nc.vector.tensor_tensor(w_lo[:, :, :], w_full[:, SPLIT[0]:SPLIT[0] + NS, :], w_hi[:, :, :].bitcast(F32),
                                    ALU.subtract).then_inc(w_parts_ready, 1)
            nc.vector.tensor_tensor(w_small_parts[QUAD:2 * QUAD, :], w_small[:, :],
                                    w_small_parts[0:QUAD, :].bitcast(F32), ALU.subtract).then_inc(w_small_lo_ready, 1)

            def product(n, s, t):
                r, u = PRODUCTS[t]
                return operands[:, s % 2, r, :], operands[:, s % 2, u, :]

            def full(n, s, j):
                if s >= 1:
                    dve.wait_ge(tile_done, tiles_through(n - 1, ("full", j)))
                a, b = product(n, s, FULL[j])
                nc.vector.tensor_tensor(full_prod[:, j, :], a, b, ALU.mult).then_inc(full_ready, 1)

            def split(n, s, j):
                if s >= 1 or j >= 2:
                    dve.wait_ge(lo_ready, n * NS + max(j - 1, 0))
                a, b = product(n, s, SPLIT[j])
                nc.vector.tensor_tensor(split_prod[:, j % 2, :], a, b, ALU.mult).then_inc(split_ready, 1)

            def low(n, s, j):
                dve.wait_ge(hi_ready, n * NS + j + 1)
                nc.vector.tensor_tensor(split_lo[:, j, :], split_prod[:, j % 2, :], split_hi[:, j, :].bitcast(F32),
                                        ALU.subtract).then_inc(lo_ready, 1)

            def step(n, s):
                dve.wait_ge(operands_loaded[s % 2], loads_through(n, s))
                full(n, s, 0)
                split(n, s, 0)
                full(n, s, 1)
                low(n, s, 0)
                split(n, s, 1)
                full(n, s, 2)
                low(n, s, 1)
                split(n, s, 2)
                if s >= 1:
                    dve.wait_ge(small_lo_ready, n)
                nc.vector.tensor_tensor(small_prod[:, :], small_operands[:, s % 2, 0, :], small_operands[:, s % 2, 1, :],
                                        ALU.mult).then_inc(small_ready, 1)
                low(n, s, 2)
                dve.wait_ge(small_hi_ready, 2 * n + 2)
                nc.vector.tensor_tensor(small_parts[2 * QUAD:3 * QUAD, :], small_prod[:, :],
                                        small_parts[0:QUAD, :].bitcast(F32), ALU.subtract).then_inc(small_lo_ready, 1)

            def loads_through(n, s):
                return (n - s % 2) * (8 * OPERAND_DMAS) + 16 * OPERAND_DMAS

            run_steps(dve, step, lambda: None)

        @block.scalar
        def _(act):
            act.wait_ge(w_loaded, W_LOADS)
            nc.scalar.copy(w_hi[:, :, :], w_full[:, SPLIT[0]:SPLIT[0] + NS, :]).then_inc(w_hi_ready, 1)
            nc.scalar.copy(w_small_parts[0:QUAD, :], w_small[:, :]).then_inc(w_hi_ready, 1)
            nc.scalar.copy(w_small_parts[2 * QUAD:3 * QUAD, :], w_small[:, :]).then_inc(w_hi_ready, 1)
            act.wait_ge(w_small_lo_ready, 1)
            nc.scalar.copy(w_small_parts[3 * QUAD:P, :], w_small_parts[QUAD:2 * QUAD, :].bitcast(F32))\
                .then_inc(w_parts_ready, 1)
            act.wait_ge(constants_ready, 3)

            def high(n, s, j):
                act.wait_ge(split_ready, n * NS + j + 1)
                if s >= 1:
                    act.wait_ge(tile_done, tiles_through(n - 1, ("split", j)))
                nc.scalar.copy(split_hi[:, j, :], split_prod[:, j % 2, :]).then_inc(hi_ready, 1)

            def take_h1(n, s):
                act.wait_ge(tile_done, n * TILES)
                if s >= 2:
                    act.wait_ge(h1_transposed, 2 * (n - 1))
                for sub in range(SUBS):
                    nc.scalar.copy(h1[:, sub * BANK:(sub + 1) * BANK], acc[(s - 1) % 2][sub][:, :]).then_inc(h1_ready, 1)

            def take_x(n, s):
                act.wait_ge(x_transposed, n)
                if s >= 2:
                    act.wait_ge(gram_done, 2 * (n - 1))
                for parity in range(2):
                    lo = parity * DIM
                    src = x_t_ps[lo:lo + DIM, 0:PER_BANK * 2 * FIELDS]\
                        .rearrange("p (t h i) -> p t h i", t=PER_BANK, h=2)
                    dst = x_diag[lo:lo + DIM, :, parity * GW:parity * GW + FIELDS]\
                        .rearrange("p (h t) i -> p t h i", h=2)
                    nc.scalar.copy(dst, src).then_inc(x_diag_ready, 1)

            def take_h1_t(n, s, half):
                act.wait_ge(h1_transposed, 2 * n - 1 + half)
                nc.scalar.copy(h1_t[:, half * PER_BANK:(half + 1) * PER_BANK, :],
                               h1_t_ps[:, :].rearrange("p (t j) -> p t j", j=HID)).then_inc(h1_t_ready, 1)

            def take_gram(n, s, half):
                act.wait_ge(gram_done, 2 * n - 1 + half)
                b0 = ((s - 1) % ROUND) * STEP_B + half * PAIRS_B
                src = gram_ps[half][:, 0:PAIRS_B * GW].rearrange("j (b c) -> j b c", c=GW)[:, :, 0:FIELDS + 1]
                dst = gram[:, :, b0:b0 + PAIRS_B].rearrange("j i b -> j b i")
                nc.scalar.copy(dst, src).then_inc(gram_ready, 1)

            def take_round(q):
                act.wait_ge(round_done, q + 1)
                nc.scalar.copy(out_sb[:, :], x_t_ps[:, 0:2 * HID]).then_inc(round_copied, 1)
                act.wait_ge(round_copied, q + 1)
                act.dma_start(out[bass.ds(q * P, P), :], out_sb[:, :]).then_inc(out_stored, 16)

            def small_high(n, s):
                act.wait_ge(small_ready, n + 1)
                if s >= 1:
                    act.wait_ge(tile_done, tiles_through(n - 1, ("small", 0)))
                nc.scalar.copy(small_parts[0:QUAD, :], small_prod[:, :]).then_inc(small_hi_ready, 1)
                nc.scalar.copy(small_parts[QUAD:2 * QUAD, :], small_prod[:, :]).then_inc(small_hi_ready, 1)

            def small_low(n, s):
                act.wait_ge(small_lo_ready, n + 1)
                nc.scalar.copy(small_parts[3 * QUAD:P, :], small_parts[2 * QUAD:3 * QUAD, :].bitcast(F32))\
                    .then_inc(small_parts_ready, 1)

            def step(n, s, q=None):
                lag = s >= 1
                if lag:
                    take_h1(n, s)
                high(n, s, 0)
                if lag:
                    take_x(n, s)
                    take_h1_t(n, s, 0)
                high(n, s, 1)
                if lag:
                    take_h1_t(n, s, 1)
                if s == ROUND + 1:
                    take_round(q)
                high(n, s, 2)
                if lag:
                    take_gram(n, s, 0)
                small_high(n, s)
                small_low(n, s)
                if lag:
                    take_gram(n, s, 1)
                if s == ROUND + 1:
                    act.wait_ge(out_stored, q * 16 + 16)

            step(0, 0)
            step(1, 1)
            with act.Fori(0, ROUNDS - 1) as q:
                for s in range(2, ROUND + 2):
                    step(q * ROUND + s, s, q)
            for s in range(2, ROUND):
                step((ROUNDS - 1) * ROUND + s, s)
            n, s = STEPS, ROUND
            take_h1(n, s)
            take_x(n, s)
            for half in range(2):
                take_h1_t(n, s, half)
            for half in range(2):
                take_gram(n, s, half)
            take_round(ROUNDS - 1)
            act.wait_ge(out_stored, ROUNDS * 16)

        @block.tensor
        def _(pe):
            pe.wait_ge(w_parts_ready, 2)
            pe.wait_ge(constants_ready, 3)

            def add(n, s, what, passes):
                first, last = PLACE[what] == 0, PLACE[what] == TILES - 1
                if first and s >= 2:
                    pe.wait_ge(h1_ready, 2 * (n - 1))
                for p, (w, z) in enumerate(passes):
                    for sub in range(SUBS):
                        done = nc.tensor.matmul(acc[s % 2][sub][:, :], w, z[:, sub * BANK:(sub + 1) * BANK],
                                                start=first and p == 0, stop=last and p == len(passes) - 1)
                done.then_inc(tile_done, 1)

            def full(n, s, j):
                pe.wait_ge(full_ready, n * len(FULL) + j + 1)
                add(n, s, ("full", j), [(w_full[:, FULL[j], :], full_prod[:, j, :])])

            def split(n, s, j):
                pe.wait_ge(lo_ready, n * NS + j + 1)
                hi, lo = split_hi[:, j, :], split_lo[:, j, :]
                add(n, s, ("split", j), [(w_hi[:, j, :], hi), (w_hi[:, j, :], lo), (w_lo[:, j, :], hi)])

            def small(n, s):
                pe.wait_ge(small_parts_ready, n + 1)
                add(n, s, ("small", 0), [(w_small_parts[:, :], small_parts[:, :])])

            def turn_x(n, s):
                p = (s - 1) % 2
                pe.wait_ge(x_nat_loaded[p], (n - 1 - p) * (8 * HALF_X) + 16 * HALF_X)
                if s >= 2:
                    pe.wait_ge(x_diag_ready, 2 * (n - 1))
                for t in range(PER_BANK):
                    done = nc.tensor.transpose(x_t_ps[:, t * 2 * FIELDS:(t + 1) * 2 * FIELDS],
                                               x_nat[:, p, 2 * t:2 * t + 2, :].rearrange("k b d -> k (b d)"),
                                               ident[0:2 * FIELDS, 0:2 * FIELDS])
                done.then_inc(x_transposed, 1)

            def turn_h1(n, s, half):
                if half == 0:
                    pe.wait_ge(h1_ready, 2 * n)
                if s >= 2 or half:
                    pe.wait_ge(h1_t_ready, 2 * (n - 1) + half)
                for t in range(PER_BANK):
                    c0 = half * BANK + t * P
                    done = nc.tensor.transpose(h1_t_ps[:, t * P:(t + 1) * P], h1[:, c0:c0 + P], ident[:, :])
                done.then_inc(h1_transposed, 1)

            def sum_gram(n, s, half):
                pe.wait_ge(h1_t_ready, 2 * n - 1 + half)
                pe.wait_ge(x_diag_ready, 2 * n)
                if s >= 2:
                    pe.wait_ge(gram_ready, 2 * (n - 1) - 1 + half)
                for t in range(PER_BANK):
                    pair = half * PER_BANK + t
                    done = nc.tensor.matmul(gram_ps[half][:, t * 2 * GW:(t + 1) * 2 * GW], h1_t[:, pair, :],
                                            x_diag[:, pair, :], start=True, stop=True)
                done.then_inc(gram_done, 1)

            def end_round(n):
                pe.wait_ge(gram_ready, 2 * n)
                nc.tensor.transpose(x_t_ps[:, 0:HID], gram[:, ONES, :], ident[:, :])
                for i in range(FIELDS):
                    done = nc.tensor.matmul(x_t_ps[:, HID:2 * HID], gram[:, i, :], w1_sb[:, i, :],
                                            start=i == 0, stop=i == FIELDS - 1)
                done.then_inc(round_done, 1)

            def step(n, s):
                lag = s >= 1
                full(n, s, 0)
                if lag:
                    turn_x(n, s)
                full(n, s, 1)
                if lag:
                    turn_h1(n, s, 0)
                if s == ROUND + 1:
                    pe.wait_ge(x_diag_ready, 2 * n)
                    end_round(n - 1)
                split(n, s, 0)
                if lag:
                    turn_h1(n, s, 1)
                full(n, s, 2)
                if lag:
                    sum_gram(n, s, 0)
                split(n, s, 1)
                if lag:
                    sum_gram(n, s, 1)
                split(n, s, 2)
                small(n, s)

            pe.wait_ge(w1_loaded, 16)
            step(0, 0)
            step(1, 1)
            with pe.Fori(0, ROUNDS - 1) as q:
                for s in range(2, ROUND + 2):
                    step(q * ROUND + s, s)
                pe.wait_ge(round_copied, q + 1)
            for s in range(2, ROUND):
                step((ROUNDS - 1) * ROUND + s, s)
            n, s = STEPS, ROUND
            turn_x(n, s)
            for half in range(2):
                turn_h1(n, s, half)
            for half in range(2):
                sum_gram(n, s, half)
            pe.wait_ge(x_diag_ready, 2 * n)
            end_round(n)


_OUT = (512, 256)


def kernel(r_x, L0_rec_W0, L0_rec_W1):
    import numpy as _np
    import concourse.bacc as _bacc
    from concourse import mybir as _mybir
    from concourse.bass_utils import run_bass_kernel_spmd as _run

    nc = _bacc.Bacc("TRN2", target_bir_lowering=False, num_devices=1)
    arrays, args = {}, []
    for name, a in (("x", r_x), ("w0", L0_rec_W0), ("w1", L0_rec_W1)):
        a = _np.ascontiguousarray(a)
        arrays[f"in_{name}"] = a
        args.append(nc.dram_tensor(f"in_{name}", a.shape, _mybir.dt.from_np(a.dtype), kind="ExternalInput").ap())
    args.append(nc.dram_tensor("out", _OUT, _mybir.dt.float32, kind="ExternalOutput").ap())
    cin_kernel(nc, *args)
    r = _run(nc, [arrays], core_ids=[0])
    return r.results[0]["out"]
```

```python
from contextlib import ExitStack

import concourse.bass as bass
from concourse import mybir

F32 = mybir.dt.float32
F32R = mybir.dt.float32r
ALU = mybir.AluOpType

PRODUCTS = [(0, 2), (2, 4), (4, 0), (0, 1), (2, 3), (1, 3)]
OFFSETS = [[19, 22, 31, 15, 27], [14, 15, 28, 9, 19], [29, 1, 12, 30, 14]]
EXTRA_START = [0, 0, 13, 13, 26]
SMALL_RUNS = [(11, 24, 3, 13), (12, 25, 3, 13), (24, 24, 15, 1), (11, 11, 2, 1)]
FULL = [0, 1, 2]
SPLIT = [3, 4, 5]
LONE = 5


def covered_pairs(fields, extra):
    seen, rows = set(), []
    for t, (r, s) in enumerate(PRODUCTS):
        for g, offset in enumerate(OFFSETS):
            for k in range(fields):
                rows.append((t, g * fields + k, (k + offset[r]) % fields, (k + offset[s]) % fields))
        for m in range(extra if t < LONE else 0):
            rows.append((t, 3 * fields + m, EXTRA_START[r] + m, EXTRA_START[s] + m))
    at = 0
    for left, right, n, step in SMALL_RUNS:
        for m in range(n):
            rows.append((6, at + m, (left + m * step) % fields, (right + m * step) % fields))
        at += n
    for row in rows:
        pair = frozenset(row[2:])
        assert pair not in seen
        seen.add(pair)
    assert len(seen) == fields * (fields + 1) // 2
    return rows


def cin_kernel(nc: bass.Bass, x: bass.AP, w0: bass.AP, w1: bass.AP, out: bass.AP):
    BATCH, FIELDS, DIM = x.shape
    HID = w0.shape[2]
    P = 128
    COLS = BATCH * DIM
    STEP = 1024
    STEP_B = STEP // DIM
    STEPS = COLS // STEP
    BANK = 512
    SUBS = STEP // BANK
    PAIRS_B = STEP_B // 2
    PER_BANK = PAIRS_B // 2
    ROUND = P // STEP_B
    ROUNDS = STEPS // ROUND
    NT = 5
    EXTRA = P - 3 * FIELDS
    SMALL = sum(run[2] for run in SMALL_RUNS)
    NS = len(SPLIT)
    TILES = len(FULL) + NS + 1
    GW = 48
    ONES = FIELDS
    PIECE_STEPS = 4
    PIECE_B = PIECE_STEPS * STEP_B
    HALF_B = PIECE_B // 2
    SUB_B = STEP_B // 2
    QUAD = 32
    covered_pairs(FIELDS, EXTRA)

    x_rows = nc.dram_tensor("x_rows", (2 * FIELDS, COLS), F32).ap()
    w_sum = nc.dram_tensor("w_sum", (2 * FIELDS, 2 * FIELDS, HID), F32).ap()
    w_sum_rows = w_sum.rearrange("u v h -> (u v) h")
    w0_rows = w0.rearrange("u v h -> (u v) h")

    ctx = ExitStack()
    with ctx:
        def sb(name, shape, dt=F32):
            return ctx.enter_context(nc.sbuf_tensor(name, shape, dt))

        def sem(name):
            return ctx.enter_context(nc.semaphore(name))

        operands = sb("operands", [P, 2, NT, STEP])
        small_operands = sb("small_operands", [QUAD, 2, 2, STEP])
        products = sb("products", [P, len(FULL) + 2, STEP])
        full_prod = products[:, 0:len(FULL), :]
        split_prod = products[:, len(FULL):len(FULL) + 2, :]
        split_hi = sb("split_hi", [P, NS, STEP], F32R)
        split_lo = sb("split_lo", [P, NS, STEP], F32R)
        small_prod = sb("small_prod", [QUAD, STEP])
        small_parts = sb("small_parts", [P, STEP], F32R)
        h1 = sb("h1", [P, STEP])
        h1_t = sb("h1_t", [P, PAIRS_B, HID])
        x_nat = sb("x_nat", [2 * FIELDS, 2, HALF_B, DIM])
        x_diag = sb("x_diag", [P, PAIRS_B, 2 * GW])
        gram = sb("gram", [P, FIELDS + 1, P])
        w1_sb = sb("w1_sb", [P, FIELDS, HID])
        w_full = sb("w_full", [P, len(PRODUCTS), HID])
        w_hi = sb("w_hi", [P, NS, HID], F32R)
        w_lo = sb("w_lo", [P, NS, HID], F32R)
        w_small = sb("w_small", [QUAD, HID])
        w_small_parts = sb("w_small_parts", [P, HID], F32R)
        w_straight = products[0:FIELDS, :, :].rearrange("u t c -> u (t c)")[:, 0:FIELDS * HID]
        w_turned = gram[0:FIELDS, 0:FIELDS, :]
        ident = sb("ident", [P, P])
        out_sb = sb("out_sb", [P, 2 * HID])

        def bank(name):
            return ctx.enter_context(nc.psum_tensor(name, [P, BANK], F32))

        acc = [[bank(f"acc{p}{s}") for s in range(SUBS)] for p in range(2)]
        h1_t_ps = bank("h1_t_ps")
        x_t_ps = bank("x_t_ps")
        gram_ps = [bank("gram_ps0"), bank("gram_ps1")]

        rows_ready = [sem("rows_ready_even"), sem("rows_ready_odd")]
        small_operands_loaded = [sem("small_operands_loaded0"), sem("small_operands_loaded1")]
        w0_loaded = sem("w0_loaded")
        w_summed = sem("w_summed")
        w_sum_stored = sem("w_sum_stored")
        w_first_loaded = sem("w_first_loaded")
        w_split_loaded = sem("w_split_loaded")
        w_small_loaded = sem("w_small_loaded")
        w_rest_loaded = sem("w_rest_loaded")
        w1_loaded = sem("w1_loaded")
        zeroed = sem("zeroed")
        pool_zeroed = sem("pool_zeroed")
        constants_ready = sem("constants_ready")
        w_hi_ready = sem("w_hi_ready")
        w_parts_ready = sem("w_parts_ready")
        w_small_lo_ready = sem("w_small_lo_ready")
        operands_loaded = [sem("operands_loaded0"), sem("operands_loaded1")]
        x_nat_loaded = [sem("x_nat_loaded0"), sem("x_nat_loaded1")]
        full_ready = sem("full_ready")
        split_ready = sem("split_ready")
        hi_ready = sem("hi_ready")
        lo_ready = sem("lo_ready")
        small_ready = sem("small_ready")
        small_hi_ready = sem("small_hi_ready")
        small_lo_ready = sem("small_lo_ready")
        small_parts_ready = sem("small_parts_ready")
        tile_done = sem("tile_done")
        h1_ready = sem("h1_ready")
        x_transposed = sem("x_transposed")
        x_diag_ready = sem("x_diag_ready")
        h1_transposed = sem("h1_transposed")
        h1_t_ready = sem("h1_t_ready")
        gram_done = sem("gram_done")
        gram_ready = sem("gram_ready")
        round_done = sem("round_done")
        round_copied = sem("round_copied")
        out_stored = sem("out_stored")

        ORDER = [("full", 0), ("split", 0), ("small", 0), ("full", 1), ("split", 1), ("split", 2), ("full", 2)]
        PLACE = {what: n for n, what in enumerate(ORDER)}

        def tiles_through(n, what):
            return n * TILES + PLACE[what] + 1

        EXTRA_LOADS = [(r, EXTRA_START.count(e)) for r, e in enumerate(EXTRA_START) if EXTRA_START.index(e) == r]
        OPERAND_DMAS = 3 * NT + len(EXTRA_LOADS)
        SMALL_DMAS = sum(1 if left == right else 2 for left, right, _, _ in SMALL_RUNS)

        def loads_through(n, s, dmas):
            return (n - s % 2) * (8 * dmas) + 16 * dmas


        def load_weight_rows(eng, done, dst, left, right, n, step=1):
            if left == right:
                src = w0_rows[left * (FIELDS + 1):(left + n - 1) * (FIELDS + 1) + 1:FIELDS + 1, :]
            else:
                first, apart = left * 2 * FIELDS + right, step * (2 * FIELDS + 1)
                src = w_sum_rows[first:first + (n - 1) * apart + 1:apart, :]
            eng.dma_start(dst, src).then_inc(done, 16)

        def load_product_weights(eng, done, t):
            r, s = PRODUCTS[t]
            for g, offset in enumerate(OFFSETS):
                load_weight_rows(eng, done, w_full[g * FIELDS:(g + 1) * FIELDS, t, :], offset[r], offset[s], FIELDS)
            if t < LONE:
                load_weight_rows(eng, done, w_full[3 * FIELDS:P, t, :], EXTRA_START[r], EXTRA_START[s], EXTRA)

        def weight_loads(tiles):
            return 16 * sum(3 + (t < LONE) for t in tiles)

        EXTRA_LOADS = [(r, EXTRA_START.count(e)) for r, e in enumerate(EXTRA_START) if EXTRA_START.index(e) == r]
        OPERAND_DMAS = 3 * NT + len(EXTRA_LOADS)
        SMALL_DMAS = sum(1 if left == right else 2 for left, right, _, _ in SMALL_RUNS)

        def loads_through(n, s, dmas):
            return (n - s % 2) * (8 * dmas) + 16 * dmas

        W_LOADS = 16 * (3 * len(PRODUCTS) + 5 + len(SMALL_RUNS))

        block = ctx.enter_context(nc.Block())

        @block.gpsimd
        def _(pool):
            def load_piece(p, parity, round_):
                for half in range(2):
                    pool.dma_start(x_nat[half * FIELDS:(half + 1) * FIELDS, parity, :, :],
                                   x[bass.ds(p * PIECE_B + half * HALF_B, HALF_B)].rearrange("b i d -> i b d"))\
                        .then_inc(x_nat_loaded[parity], 16)

            def store_piece(p, parity, round_):
                pool.wait_ge(x_nat_loaded[parity], round_ * 32 + 32)
                for copy in range(2):
                    for half in range(2):
                        dst = x_rows[copy * FIELDS:(copy + 1) * FIELDS, bass.ds(p * (PIECE_B * DIM), PIECE_B * DIM)]\
                            .rearrange("k (s h c) -> k s h c", h=2, c=BANK)[:, :, half, :]
                        src = x_nat[half * FIELDS:(half + 1) * FIELDS, parity, :, :]\
                            .rearrange("k (s b) d -> k s (b d)", b=SUB_B)
                        pool.dma_start(dst, src).then_inc(rows_ready[parity], 16)

            load_piece(0, 0, 0)
            nc.gpsimd.memset(small_operands[:, :, :, :], 0.0).then_inc(pool_zeroed, 1)
            nc.gpsimd.memset(ident[:, :], 0.0).then_inc(pool_zeroed, 1)
            store_piece(0, 0, 0)
            nc.gpsimd.memset(x_diag[:, :, :], 0.0).then_inc(pool_zeroed, 1)
            pool.wait_ge(pool_zeroed, 3)
            nc.gpsimd.affine_select(out=ident[:, :], in_=ident[:, :], compare_op=ALU.not_equal, fill=1.0, base=0,
                                    pattern=[[-1, P]], channel_multiplier=1).then_inc(constants_ready, 1)
            pool.wait_ge(constants_ready, 1)
            nc.gpsimd.memset(x_diag[0:DIM, :, ONES:ONES + 1], 1.0).then_inc(constants_ready, 1)
            nc.gpsimd.memset(x_diag[DIM:P, :, GW + ONES:GW + ONES + 1], 1.0).then_inc(constants_ready, 1)
            pool.wait_ge(w_sum_stored, 64)
            pool.wait_ge(zeroed, 2)
            at = 0
            for left, right, rows, step in SMALL_RUNS:
                load_weight_rows(pool, w_small_loaded, w_small[at:at + rows, :], left, right, rows, step)
                at += rows
            for t in FULL[1:]:
                load_product_weights(pool, w_rest_loaded, t)
            load_piece(1, 1, 0)
            store_piece(1, 1, 0)
            with pool.Fori(1, ROUNDS) as q:
                for parity in range(2):
                    pool.wait_ge(x_transposed, (q - 1) * ROUND + (parity + 1) * PIECE_STEPS)
                    pool.wait_ge(rows_ready[parity], q * 64)
                    load_piece(q * 2 + parity, parity, q)
                    pool.wait_ge(x_transposed, (q - 1) * ROUND + (parity + 1) * PIECE_STEPS + 1)
                    store_piece(q * 2 + parity, parity, q)

        @block.sync
        def _(sp):
            sp.dma_start(w_straight[:, :], w0.rearrange("u v h -> u (v h)")).then_inc(w0_loaded, 16)
            sp.dma_start(w_turned, w0.rearrange("u v h -> v u h")).then_inc(w0_loaded, 16)

            def load_operands(n, s, round_):
                piece_in_round = (s % ROUND) // PIECE_STEPS
                if s >= 2:
                    sp.wait_ge(full_ready, (n - 1) * len(FULL))
                sp.wait_ge(rows_ready[piece_in_round], round_ * 64 + 64)
                c0 = n * STEP
                for r in range(NT):
                    for g in range(3):
                        a = OFFSETS[g][r]
                        sp.dma_start(operands[g * FIELDS:(g + 1) * FIELDS, s % 2, r, :],
                                     x_rows[a:a + FIELDS, bass.ds(c0, STEP)]).then_inc(operands_loaded[s % 2], 16)
                for r, same in EXTRA_LOADS:
                    a = EXTRA_START[r]
                    sp.dma_start(operands[3 * FIELDS:P, s % 2, r:r + same, :], rows_twice(a, EXTRA, 1, c0, same))\
                        .then_inc(operands_loaded[s % 2], 16)

            def rows_twice(row, rows, step, c0, times):
                src = x_rows[row:row + (rows - 1) * step + 1:step, bass.ds(c0, STEP)]
                return src.unsqueeze(1).broadcast_to((rows, times, STEP))

            def load_small(n, s):
                if s >= 2:
                    sp.wait_ge(small_ready, n - 1)
                at = 0
                for left, right, rows, step in SMALL_RUNS:
                    if left == right:
                        sp.dma_start(small_operands[at:at + rows, s % 2, :, :], rows_twice(left, rows, step, n * STEP, 2))\
                            .then_inc(small_operands_loaded[s % 2], 16)
                    else:
                        for side, row in ((0, left), (1, right)):
                            sp.dma_start(small_operands[at:at + rows, s % 2, side, :],
                                         x_rows[row:row + (rows - 1) * step + 1:step, bass.ds(n * STEP, STEP)])\
                                .then_inc(small_operands_loaded[s % 2], 16)
                    at += rows

            def store_weight_sums():
                sp.wait_ge(w_summed, 1)
                for u in range(2):
                    for v in range(2):
                        sp.dma_start(w_sum[u * FIELDS:(u + 1) * FIELDS, v * FIELDS:(v + 1) * FIELDS, :],
                                     w_straight[:, :].rearrange("u (v h) -> u v h", h=HID)).then_inc(w_sum_stored, 16)

            store_weight_sums()
            load_operands(0, 0, 0)
            sp.wait_ge(pool_zeroed, 2)
            load_small(0, 0)
            sp.wait_ge(w_sum_stored, 64)
            sp.wait_ge(zeroed, 2)
            load_product_weights(sp, w_first_loaded, FULL[0])
            for t in SPLIT:
                load_product_weights(sp, w_split_loaded, t)
            load_operands(1, 1, 0)
            load_small(1, 1)
            sp.dma_start(w1_sb[:, :, :], w1.rearrange("i j h -> j i h")).then_inc(w1_loaded, 16)
            with sp.Fori(0, ROUNDS - 1) as q:
                for s in range(2, ROUND + 2):
                    load_operands(q * ROUND + s, s, q + s // ROUND)
                    load_small(q * ROUND + s, s)
            for s in range(2, ROUND):
                load_operands((ROUNDS - 1) * ROUND + s, s, ROUNDS - 1)
                load_small((ROUNDS - 1) * ROUND + s, s)

        @block.vector
        def _(dve):
            nc.vector.memset(w_full[:, :, :], 0.0).then_inc(zeroed, 1)
            nc.vector.memset(w_small[:, :], 0.0).then_inc(zeroed, 1)
            dve.wait_ge(w0_loaded, 32)
            nc.vector.tensor_tensor(w_straight[:, :], w_straight[:, :], w_turned.rearrange("u v h -> u (v h)"),
                                    ALU.add).then_inc(w_summed, 1)
            dve.wait_ge(w_sum_stored, 64)

            def split_weights():
                dve.wait_ge(w_hi_ready, 3)
                nc.vector.tensor_tensor(w_lo[:, :, :], w_full[:, SPLIT[0]:SPLIT[0] + NS, :], w_hi[:, :, :].bitcast(F32),
                                        ALU.subtract).then_inc(w_parts_ready, 1)
                nc.vector.tensor_tensor(w_small_parts[QUAD:2 * QUAD, :], w_small[:, :],
                                        w_small_parts[0:QUAD, :].bitcast(F32), ALU.subtract).then_inc(w_small_lo_ready, 1)

            def product(n, s, t):
                r, u = PRODUCTS[t]
                return operands[:, s % 2, r, :], operands[:, s % 2, u, :]

            def full(n, s, j):
                if s >= 1:
                    dve.wait_ge(tile_done, tiles_through(n - 1, ("full", j)))
                a, b = product(n, s, FULL[j])
                nc.vector.tensor_tensor(full_prod[:, j, :], a, b, ALU.mult).then_inc(full_ready, 1)

            def split(n, s, j):
                if s >= 1 or j >= 2:
                    dve.wait_ge(lo_ready, n * NS + max(j - 1, 0))
                a, b = product(n, s, SPLIT[j])
                nc.vector.tensor_tensor(split_prod[:, j % 2, :], a, b, ALU.mult).then_inc(split_ready, 1)

            def low(n, s, j):
                dve.wait_ge(hi_ready, n * NS + j + 1)
                nc.vector.tensor_tensor(split_lo[:, j, :], split_prod[:, j % 2, :], split_hi[:, j, :].bitcast(F32),
                                        ALU.subtract).then_inc(lo_ready, 1)

            def small(n, s):
                dve.wait_ge(small_operands_loaded[s % 2], loads_through(n, s, SMALL_DMAS))
                if s >= 1:
                    dve.wait_ge(small_lo_ready, n)
                nc.vector.tensor_tensor(small_prod[:, :], small_operands[:, s % 2, 0, :], small_operands[:, s % 2, 1, :],
                                        ALU.mult).then_inc(small_ready, 1)

            def small_low(n, s):
                dve.wait_ge(small_hi_ready, 2 * n + 2)
                nc.vector.tensor_tensor(small_parts[2 * QUAD:3 * QUAD, :], small_prod[:, :],
                                        small_parts[0:QUAD, :].bitcast(F32), ALU.subtract).then_inc(small_lo_ready, 1)

            def step(n, s):
                dve.wait_ge(operands_loaded[s % 2], loads_through(n, s, OPERAND_DMAS))
                full(n, s, 0)
                split(n, s, 0)
                small(n, s)
                if s == 0:
                    split_weights()
                low(n, s, 0)
                split(n, s, 1)
                small_low(n, s)
                split(n, s, 2)
                full(n, s, 1)
                low(n, s, 1)
                low(n, s, 2)
                full(n, s, 2)

            step(0, 0)
            step(1, 1)
            with dve.Fori(0, ROUNDS - 1) as q:
                for s in range(2, ROUND + 2):
                    step(q * ROUND + s, s)
            for s in range(2, ROUND):
                step((ROUNDS - 1) * ROUND + s, s)

        @block.scalar
        def _(act):
            act.wait_ge(w_split_loaded, weight_loads(SPLIT))
            nc.scalar.copy(w_hi[:, :, :], w_full[:, SPLIT[0]:SPLIT[0] + NS, :]).then_inc(w_hi_ready, 1)
            act.wait_ge(w_small_loaded, 16 * len(SMALL_RUNS))
            nc.scalar.copy(w_small_parts[0:QUAD, :], w_small[:, :]).then_inc(w_hi_ready, 1)
            nc.scalar.copy(w_small_parts[2 * QUAD:3 * QUAD, :], w_small[:, :]).then_inc(w_hi_ready, 1)
            act.wait_ge(w_small_lo_ready, 1)
            nc.scalar.copy(w_small_parts[3 * QUAD:P, :], w_small_parts[QUAD:2 * QUAD, :].bitcast(F32))\
                .then_inc(w_parts_ready, 1)
            act.wait_ge(constants_ready, 3)

            def high(n, s, j):
                act.wait_ge(split_ready, n * NS + j + 1)
                if s >= 1:
                    act.wait_ge(tile_done, tiles_through(n - 1, ("split", j)))
                nc.scalar.copy(split_hi[:, j, :], split_prod[:, j % 2, :]).then_inc(hi_ready, 1)

            def take_h1(n, s):
                act.wait_ge(tile_done, n * TILES)
                if s >= 2:
                    act.wait_ge(h1_transposed, 2 * (n - 1))
                for sub in range(SUBS):
                    nc.scalar.copy(h1[:, sub * BANK:(sub + 1) * BANK], acc[(s - 1) % 2][sub][:, :]).then_inc(h1_ready, 1)

            def take_x(n, s):
                act.wait_ge(x_transposed, n)
                if s >= 2:
                    act.wait_ge(gram_done, 2 * (n - 1))
                for parity in range(2):
                    lo = parity * DIM
                    src = x_t_ps[lo:lo + DIM, 0:PER_BANK * 2 * FIELDS]\
                        .rearrange("p (t h i) -> p t h i", t=PER_BANK, h=2)
                    dst = x_diag[lo:lo + DIM, :, parity * GW:parity * GW + FIELDS]\
                        .rearrange("p (h t) i -> p t h i", h=2)
                    nc.scalar.copy(dst, src).then_inc(x_diag_ready, 1)

            def take_h1_t(n, s, half):
                act.wait_ge(h1_transposed, 2 * n - 1 + half)
                nc.scalar.copy(h1_t[:, half * PER_BANK:(half + 1) * PER_BANK, :],
                               h1_t_ps[:, :].rearrange("p (t j) -> p t j", j=HID)).then_inc(h1_t_ready, 1)

            def take_gram(n, s, half):
                act.wait_ge(gram_done, 2 * n - 1 + half)
                piece, in_piece = divmod((s - 1) % ROUND, PIECE_STEPS)
                b0 = piece * PIECE_B + half * HALF_B + in_piece * SUB_B
                src = gram_ps[half][:, 0:PAIRS_B * GW].rearrange("j (b c) -> j b c", c=GW)[:, :, 0:FIELDS + 1]
                dst = gram[:, :, b0:b0 + PAIRS_B].rearrange("j i b -> j b i")
                nc.scalar.copy(dst, src).then_inc(gram_ready, 1)

            def take_round(q):
                act.wait_ge(round_done, q + 1)
                nc.scalar.copy(out_sb[:, :], x_t_ps[:, 0:2 * HID]).then_inc(round_copied, 1)
                act.wait_ge(round_copied, q + 1)
                act.dma_start(out[bass.ds(q * P, P), :], out_sb[:, :]).then_inc(out_stored, 16)

            def small_high(n, s):
                act.wait_ge(small_ready, n + 1)
                if s >= 1:
                    act.wait_ge(tile_done, tiles_through(n - 1, ("small", 0)))
                nc.scalar.copy(small_parts[0:QUAD, :], small_prod[:, :]).then_inc(small_hi_ready, 1)
                nc.scalar.copy(small_parts[QUAD:2 * QUAD, :], small_prod[:, :]).then_inc(small_hi_ready, 1)

            def small_low(n, s):
                act.wait_ge(small_lo_ready, n + 1)
                nc.scalar.copy(small_parts[3 * QUAD:P, :], small_parts[2 * QUAD:3 * QUAD, :].bitcast(F32))\
                    .then_inc(small_parts_ready, 1)

            def step(n, s, q=None, lag=True, ahead=True):
                if lag:
                    take_h1(n, s)
                    take_x(n, s)
                    take_h1_t(n, s, 0)
                if ahead:
                    high(n + 1, s + 1, 0)
                    small_high(n + 1, s + 1)
                if lag:
                    take_h1_t(n, s, 1)
                if s == ROUND + 1:
                    take_round(q)
                if ahead:
                    small_low(n + 1, s + 1)
                    high(n + 1, s + 1, 1)
                if lag:
                    take_gram(n, s, 0)
                if ahead:
                    high(n + 1, s + 1, 2)
                if lag:
                    take_gram(n, s, 1)
                if s == ROUND + 1:
                    act.wait_ge(out_stored, q * 16 + 16)

            step(-1, -1, lag=False)
            step(0, 0, lag=False)
            step(1, 1)
            with act.Fori(0, ROUNDS - 1) as q:
                for s in range(2, ROUND + 2):
                    step(q * ROUND + s, s, q)
            for s in range(2, ROUND + 1):
                step((ROUNDS - 1) * ROUND + s, s, ahead=s < ROUND - 1)
            take_round(ROUNDS - 1)
            act.wait_ge(out_stored, ROUNDS * 16)

        @block.tensor
        def _(pe):
            def add(n, s, what, passes):
                first, last = PLACE[what] == 0, PLACE[what] == TILES - 1
                if first and s >= 2:
                    pe.wait_ge(h1_ready, 2 * (n - 1))
                for p, (w, z) in enumerate(passes):
                    for sub in range(SUBS):
                        done = nc.tensor.matmul(acc[s % 2][sub][:, :], w, z[:, sub * BANK:(sub + 1) * BANK],
                                                start=first and p == 0, stop=last and p == len(passes) - 1)
                done.then_inc(tile_done, 1)

            def full(n, s, j):
                pe.wait_ge(full_ready, n * len(FULL) + j + 1)
                add(n, s, ("full", j), [(w_full[:, FULL[j], :], full_prod[:, j, :])])

            def split(n, s, j):
                pe.wait_ge(lo_ready, n * NS + j + 1)
                hi, lo = split_hi[:, j, :], split_lo[:, j, :]
                add(n, s, ("split", j), [(w_hi[:, j, :], hi), (w_hi[:, j, :], lo), (w_lo[:, j, :], hi)])

            def small(n, s):
                pe.wait_ge(small_parts_ready, n + 1)
                add(n, s, ("small", 0), [(w_small_parts[:, :], small_parts[:, :])])

            def turn_x(n, s, q):
                piece, in_piece = divmod((s - 1) % ROUND, PIECE_STEPS)
                if in_piece == 0:
                    pe.wait_ge(x_nat_loaded[piece], (q + (s - 1) // ROUND) * 32 + 32)
                if s >= 2:
                    pe.wait_ge(x_diag_ready, 2 * (n - 1))
                for t in range(PER_BANK):
                    b = in_piece * SUB_B + 2 * t
                    done = nc.tensor.transpose(x_t_ps[:, t * 2 * FIELDS:(t + 1) * 2 * FIELDS],
                                               x_nat[:, piece, b:b + 2, :].rearrange("k b d -> k (b d)"),
                                               ident[0:2 * FIELDS, 0:2 * FIELDS])
                done.then_inc(x_transposed, 1)

            def turn_h1(n, s, half):
                if half == 0:
                    pe.wait_ge(h1_ready, 2 * n)
                if s >= 2 or half:
                    pe.wait_ge(h1_t_ready, 2 * (n - 1) + half)
                for t in range(PER_BANK):
                    c0 = half * BANK + t * P
                    done = nc.tensor.transpose(h1_t_ps[:, t * P:(t + 1) * P], h1[:, c0:c0 + P], ident[:, :])
                done.then_inc(h1_transposed, 1)

            def sum_gram(n, s, half):
                pe.wait_ge(h1_t_ready, 2 * n - 1 + half)
                pe.wait_ge(x_diag_ready, 2 * n)
                if s >= 2:
                    pe.wait_ge(gram_ready, 2 * (n - 1) - 1 + half)
                for t in range(PER_BANK):
                    pair = half * PER_BANK + t
                    done = nc.tensor.matmul(gram_ps[half][:, t * 2 * GW:(t + 1) * 2 * GW], h1_t[:, pair, :],
                                            x_diag[:, pair, :], start=True, stop=True)
                done.then_inc(gram_done, 1)

            def end_round(n):
                pe.wait_ge(gram_ready, 2 * n)
                nc.tensor.transpose(x_t_ps[:, 0:HID], gram[:, ONES, :], ident[:, :])
                for i in range(FIELDS):
                    done = nc.tensor.matmul(x_t_ps[:, HID:2 * HID], gram[:, i, :], w1_sb[:, i, :],
                                            start=i == 0, stop=i == FIELDS - 1)
                done.then_inc(round_done, 1)

            def step(n, s, q):
                lag = s >= 1
                if s == 0:
                    pe.wait_ge(w_first_loaded, weight_loads(FULL[:1]))
                full(n, s, 0)
                if lag:
                    turn_x(n, s, q)
                if s == 0:
                    pe.wait_ge(w_parts_ready, 2)
                split(n, s, 0)
                if lag:
                    turn_h1(n, s, 0)
                small(n, s)
                if s == ROUND + 1:
                    pe.wait_ge(x_diag_ready, 2 * n)
                    end_round(n - 1)
                if s == 0:
                    pe.wait_ge(w_rest_loaded, weight_loads(FULL[1:]))
                full(n, s, 1)
                if lag:
                    turn_h1(n, s, 1)
                split(n, s, 1)
                if lag:
                    sum_gram(n, s, 0)
                split(n, s, 2)
                if lag:
                    sum_gram(n, s, 1)
                full(n, s, 2)

            step(0, 0, 0)
            pe.wait_ge(constants_ready, 3)
            step(1, 1, 0)
            pe.wait_ge(w1_loaded, 16)
            with pe.Fori(0, ROUNDS - 1) as q:
                for s in range(2, ROUND + 2):
                    step(q * ROUND + s, s, q)
                pe.wait_ge(round_copied, q + 1)
            for s in range(2, ROUND):
                step((ROUNDS - 1) * ROUND + s, s, ROUNDS - 1)
            n, s = STEPS, ROUND
            turn_x(n, s, ROUNDS - 1)
            for half in range(2):
                turn_h1(n, s, half)
            for half in range(2):
                sum_gram(n, s, half)
            pe.wait_ge(x_diag_ready, 2 * n)
            end_round(n)


_OUT = (512, 256)


def kernel(r_x, L0_rec_W0, L0_rec_W1):
    import numpy as _np
    import concourse.bacc as _bacc
    from concourse import mybir as _mybir
    from concourse.bass_utils import run_bass_kernel_spmd as _run

    nc = _bacc.Bacc("TRN2", target_bir_lowering=False, num_devices=1)
    arrays, args = {}, []
    for name, a in (("x", r_x), ("w0", L0_rec_W0), ("w1", L0_rec_W1)):
        a = _np.ascontiguousarray(a)
        arrays[f"in_{name}"] = a
        args.append(nc.dram_tensor(f"in_{name}", a.shape, _mybir.dt.from_np(a.dtype), kind="ExternalInput").ap())
    args.append(nc.dram_tensor("out", _OUT, _mybir.dt.float32, kind="ExternalOutput").ap())
    cin_kernel(nc, *args)
    r = _run(nc, [arrays], core_ids=[0])
    return r.results[0]["out"]
```

```python
from contextlib import ExitStack

import concourse.bass as bass
from concourse import mybir

F32 = mybir.dt.float32
F32R = mybir.dt.float32r
ALU = mybir.AluOpType

PRODUCTS = [(0, 2), (2, 4), (4, 0), (0, 1), (2, 3), (1, 3)]
OFFSETS = [[19, 22, 31, 15, 27], [14, 15, 28, 9, 19], [29, 1, 12, 30, 14]]
EXTRA_START = [0, 0, 13, 13, 26]
THIRD = 13
SMALL_PAIRS = (11, 3, 2)
SMALL_SQUARES = [(24, 15), (11, 2)]
LOAD_GROUPS = [(0, 2), (1, 3), (4,)]
FULL = [0, 1, 2]
SPLIT = [3, 4, 5]
LONE = 5


def pair_places(fields):
    extra = 128 - 3 * fields
    groups = [[((k + offset[r]) % fields, (k + offset[s]) % fields) for r, s in PRODUCTS]
              for offset in OFFSETS for k in range(fields)]
    extras = [[(EXTRA_START[r] + m, EXTRA_START[s] + m) for r, s in PRODUCTS[:LONE]] for m in range(extra)]
    first, thirds, width = SMALL_PAIRS
    small = [((first + m * THIRD + e) % fields, (first + (m + 1) * THIRD + e) % fields)
             for m in range(thirds) for e in range(width)]
    small += [(start + m, start + m) for start, n in SMALL_SQUARES for m in range(n)]
    every = [frozenset(pair) for row in groups + extras for pair in row] + [frozenset(pair) for pair in small]
    assert len(every) == len(set(every)) == fields * (fields + 1) // 2
    return groups, extras, small


def cin_kernel(nc: bass.Bass, x_fields: bass.AP, x_small: bass.AP, x_dims: bass.AP, w_groups: bass.AP, w_extras: bass.AP,
               w_small: bass.AP, w1: bass.AP, out: bass.AP):
    P, PAIRS, FIELDS = x_dims.shape
    HID = w1.shape[2]
    DIM = P // 2
    COLS = 2 * PAIRS * DIM
    STEP = 1024
    STEP_B = STEP // DIM
    STEPS = COLS // STEP
    BANK = 512
    SUBS = STEP // BANK
    PAIRS_B = STEP_B // 2
    PER_BANK = PAIRS_B // 2
    ROUND = P // STEP_B
    ROUNDS = STEPS // ROUND
    NT = 5
    EXTRA = P - 3 * FIELDS
    SMALL = w_small.shape[1]
    SMALL_MIXED = SMALL_PAIRS[1] * SMALL_PAIRS[2]
    NS = len(SPLIT)
    TILES = len(FULL) + NS + 1
    GW = 48
    ONES = FIELDS
    PIECE_STEPS = 4
    PIECE_PAIRS = PIECE_STEPS * PAIRS_B
    QUAD = 32
    W1_PARTS = 3
    assert FIELDS % W1_PARTS == 0
    SQUARE_TILES = [t for t, (r, s) in enumerate(PRODUCTS[:LONE]) if EXTRA_START[r] == EXTRA_START[s]]
    MIXED_TILES = SQUARE_TILES[0]
    assert SQUARE_TILES == list(range(MIXED_TILES, LONE))

    ctx = ExitStack()
    with ctx:
        def sb(name, shape, dt=F32):
            return ctx.enter_context(nc.sbuf_tensor(name, shape, dt))

        def sem(name):
            return ctx.enter_context(nc.semaphore(name))

        operands = sb("operands", [P, 2, NT, STEP])
        small_operands = sb("small_operands", [P, 2, 2, STEP])
        products = sb("products", [P, len(FULL) + 2, STEP])
        full_prod = products[:, 0:len(FULL), :]
        split_prod = products[:, len(FULL):len(FULL) + 2, :]
        split_hi = sb("split_hi", [P, NS, STEP], F32R)
        split_lo = sb("split_lo", [P, NS, STEP], F32R)
        small_prod = sb("small_prod", [P, STEP])
        small_parts = sb("small_parts", [P, 2, STEP], F32R)
        h1 = sb("h1", [P, STEP])
        h1_t = sb("h1_t", [P, PAIRS_B, HID])
        x_turned = sb("x_turned", [P, 2, PIECE_PAIRS, FIELDS])
        x_diag = sb("x_diag", [P, PAIRS_B, 2 * GW])
        gram = sb("gram", [P, FIELDS + 1, P])
        w1_sb = sb("w1_sb", [P, FIELDS, HID])
        w_full = sb("w_full", [P, len(PRODUCTS), HID])
        w_hi = sb("w_hi", [P, NS, HID], F32R)
        w_lo = sb("w_lo", [P, NS, HID], F32R)
        w_small_sum = sb("w_small_sum", [QUAD, HID])
        w_small_parts = sb("w_small_parts", [P, HID], F32R)
        w_back = gram[:, 0:len(PRODUCTS), :]
        w_small_back = gram[0:QUAD, len(PRODUCTS), :]
        ident = sb("ident", [P, P])
        out_sb = sb("out_sb", [P, 2 * HID])

        def bank(name):
            return ctx.enter_context(nc.psum_tensor(name, [P, BANK], F32))

        acc = [[bank(f"acc{p}{s}") for s in range(SUBS)] for p in range(2)]
        h1_t_ps = bank("h1_t_ps")
        out_ps = bank("out_ps")
        gram_ps = [bank("gram_ps0"), bank("gram_ps1")]

        zeroed = sem("zeroed")
        small_zeroed = sem("small_zeroed")
        ident_zeroed = sem("ident_zeroed")
        ident_ready = sem("ident_ready")
        diag_zeroed = sem("diag_zeroed")
        diag_ready = sem("diag_ready")
        w_loaded = sem("w_loaded")
        w_small_loaded = sem("w_small_loaded")
        w_summed = sem("w_summed")
        w_small_summed = sem("w_small_summed")
        w_hi_ready = sem("w_hi_ready")
        w_lo_ready = sem("w_lo_ready")
        w_small_hi_ready = sem("w_small_hi_ready")
        w_small_lo_ready = sem("w_small_lo_ready")
        w1_loaded = sem("w1_loaded")
        operands_loaded = [[sem(f"operands{''.join(map(str, tiles))}_loaded{p}") for p in range(2)]
                           for tiles in LOAD_GROUPS]
        small_operands_loaded = [sem("small_operands_loaded0"), sem("small_operands_loaded1")]
        first_odd_loaded = sem("first_odd_loaded")
        x_turned_loaded = [sem("x_turned_loaded0"), sem("x_turned_loaded1")]
        full_ready = sem("full_ready")
        split_ready = sem("split_ready")
        hi_ready = sem("hi_ready")
        lo_ready = sem("lo_ready")
        small_ready = sem("small_ready")
        small_hi_ready = sem("small_hi_ready")
        small_lo_ready = sem("small_lo_ready")
        tile_done = sem("tile_done")
        h1_ready = sem("h1_ready")
        x_diag_ready = sem("x_diag_ready")
        h1_transposed = sem("h1_transposed")
        h1_t_ready = sem("h1_t_ready")
        gram_done = sem("gram_done")
        gram_ready = sem("gram_ready")
        round_done = sem("round_done")
        round_copied = sem("round_copied")
        out_stored = sem("out_stored")

        ORDER = [("full", 0), ("split", 0), ("full", 1), ("split", 1), ("small", 0), ("split", 2), ("full", 2)]
        PLACE = {what: n for n, what in enumerate(ORDER)}

        def tiles_through(n, what):
            return n * TILES + PLACE[what] + 1

        def load_group_dmas(tiles):
            return 3 * len(tiles) + sum(EXTRA_START.index(EXTRA_START[r]) == r for r in tiles)

        def loads_through(n, s, dmas):
            return (n - s % 2) * (8 * dmas) + 16 * dmas

        SMALL_DMAS = 2

        block = ctx.enter_context(nc.Block())

        def load_small(eng, done, n, s):
            c0 = n * STEP
            for copy in range(2):
                at = (s % 2) * 2 * QUAD + copy * QUAD
                eng.dma_start(small_operands[at:at + SMALL, (s // 2) % 2, :, :], x_small[:, :, bass.ds(c0, STEP)])\
                    .then_inc(done, 16)

        def rows_for(row, rows, c0, times):
            return x_fields[row:row + rows, bass.ds(c0, STEP)].unsqueeze(1).broadcast_to((rows, times, STEP))

        @block.gpsimd
        def _(pool):
            pool.wait_ge(zeroed, 2)
            for dst, way, mixed in ((w_full, 0, LONE), (w_back, 1, MIXED_TILES)):
                pool.dma_start(dst[0:3 * FIELDS, :, :], w_groups[way]).then_inc(w_loaded, 16)
                pool.dma_start(dst[3 * FIELDS:P, 0:mixed, :], w_extras[way, :, 0:mixed, :]).then_inc(w_loaded, 16)
            nc.gpsimd.memset(ident[:, :], 0.0).then_inc(ident_zeroed, 1)
            pool.wait_ge(ident_zeroed, 1)
            nc.gpsimd.affine_select(out=ident[:, :], in_=ident[:, :], compare_op=ALU.not_equal, fill=1.0, base=0,
                                    pattern=[[-1, P]], channel_multiplier=1).then_inc(ident_ready, 1)
            pool.wait_ge(small_zeroed, 3)
            pool.dma_start(w_small_sum[0:SMALL, :], w_small[0]).then_inc(w_small_loaded, 16)
            pool.dma_start(w_small_back[0:SMALL_MIXED, :], w_small[1, 0:SMALL_MIXED, :]).then_inc(w_small_loaded, 16)
            load_small(pool, first_odd_loaded, 1, 1)
            nc.gpsimd.memset(x_diag[:, :, :], 0.0).then_inc(diag_zeroed, 1)
            pool.wait_ge(diag_zeroed, 1)
            nc.gpsimd.memset(x_diag[0:DIM, :, ONES:ONES + 1], 1.0).then_inc(diag_ready, 1)
            nc.gpsimd.memset(x_diag[DIM:P, :, GW + ONES:GW + ONES + 1], 1.0).then_inc(diag_ready, 1)

            def load_piece(q, parity):
                pool.dma_start(x_turned[:, parity, :, :],
                               x_dims[:, bass.ds(q * (2 * PIECE_PAIRS) + parity * PIECE_PAIRS, PIECE_PAIRS), :])\
                    .then_inc(x_turned_loaded[parity], 16)

            load_piece(0, 0)
            load_piece(0, 1)
            for part in range(W1_PARTS):
                if part:
                    pool.wait_ge(x_diag_ready, 4 * part)
                i0 = part * (FIELDS // W1_PARTS)
                pool.dma_start(w1_sb[:, i0:i0 + FIELDS // W1_PARTS, :],
                               w1[i0:i0 + FIELDS // W1_PARTS].rearrange("i j h -> j i h")).then_inc(w1_loaded, 16)
            with pool.Fori(1, ROUNDS) as q:
                for parity in range(2):
                    pool.wait_ge(x_diag_ready, q * (2 * ROUND) + 2 * ((parity + 1) * PIECE_STEPS - ROUND))
                    load_piece(q, parity)

        @block.sync
        def _(sp):
            def load_group(n, s, group):
                if s >= 2:
                    sp.wait_ge(full_ready, (n - 1) * len(FULL))
                done = operands_loaded[group][s % 2]
                c0 = n * STEP
                for r in LOAD_GROUPS[group]:
                    for g in range(3):
                        a = OFFSETS[g][r]
                        sp.dma_start(operands[g * FIELDS:(g + 1) * FIELDS, s % 2, r, :],
                                     x_fields[a:a + FIELDS, bass.ds(c0, STEP)]).then_inc(done, 16)
                    if EXTRA_START.index(EXTRA_START[r]) == r:
                        same = EXTRA_START.count(EXTRA_START[r])
                        sp.dma_start(operands[3 * FIELDS:P, s % 2, r:r + same, :],
                                     rows_for(EXTRA_START[r], EXTRA, c0, same)).then_inc(done, 16)

            def load_step(n, s, small=True):
                for group in range(len(LOAD_GROUPS)):
                    load_group(n, s, group)
                if small:
                    if s >= 3 and s % 2 == 1:
                        sp.wait_ge(small_ready, n - 1)
                    load_small(sp, small_operands_loaded[((s + 1) // 2) % 2], n + 1, s + 1)

            load_group(0, 0, 0)
            load_group(0, 0, 1)
            sp.wait_ge(small_zeroed, 3)
            load_small(sp, small_operands_loaded[0], 0, 0)
            load_group(0, 0, 2)
            load_step(1, 1)
            load_step(2, 2)
            with sp.Fori(0, ROUNDS - 1) as q:
                for s in range(3, ROUND + 3):
                    load_step(q * ROUND + s, s)
            for s in range(3, ROUND):
                load_step((ROUNDS - 1) * ROUND + s, s, small=s < ROUND - 1)

        def small_halves(s):
            even, odd = slice(0, 2 * QUAD), slice(2 * QUAD, P)
            return (even, odd) if s % 2 == 0 else (odd, even)

        @block.vector
        def _(dve):
            nc.vector.memset(w_full[:, :, :], 0.0).then_inc(zeroed, 1)
            nc.vector.memset(w_back, 0.0).then_inc(zeroed, 1)
            nc.vector.memset(w_small_sum[:, :], 0.0).then_inc(small_zeroed, 1)
            nc.vector.memset(w_small_back, 0.0).then_inc(small_zeroed, 1)
            nc.vector.memset(small_operands[:, :, :, :], 0.0).then_inc(small_zeroed, 1)

            def sum_weights():
                dve.wait_ge(w_loaded, 64)
                nc.vector.tensor_tensor(w_full[:, :, :], w_full[:, :, :], w_back, ALU.add).then_inc(w_summed, 1)
                dve.wait_ge(w_small_loaded, 32)
                nc.vector.tensor_tensor(w_small_sum[:, :], w_small_sum[:, :], w_small_back, ALU.add)\
                    .then_inc(w_small_summed, 1)

            def split_weights():
                dve.wait_ge(w_hi_ready, 1)
                nc.vector.tensor_tensor(w_lo[:, :, :], w_full[:, SPLIT[0]:SPLIT[0] + NS, :], w_hi[:, :, :].bitcast(F32),
                                        ALU.subtract).then_inc(w_lo_ready, 1)
                dve.wait_ge(w_small_hi_ready, 2)
                for at in (QUAD, 3 * QUAD):
                    nc.vector.tensor_tensor(w_small_parts[at:at + QUAD, :], w_small_sum[:, :],
                                            w_small_parts[0:QUAD, :].bitcast(F32), ALU.subtract)\
                        .then_inc(w_small_lo_ready, 1)

            def product(n, s, t):
                r, u = PRODUCTS[t]
                return operands[:, s % 2, r, :], operands[:, s % 2, u, :]

            def full(n, s, j):
                if s >= 1:
                    dve.wait_ge(tile_done, tiles_through(n - 1, ("full", j)))
                a, b = product(n, s, FULL[j])
                nc.vector.tensor_tensor(full_prod[:, j, :], a, b, ALU.mult).then_inc(full_ready, 1)

            def split(n, s, j):
                if s >= 1 or j >= 2:
                    dve.wait_ge(lo_ready, n * NS + max(j - 1, 0))
                a, b = product(n, s, SPLIT[j])
                nc.vector.tensor_tensor(split_prod[:, j % 2, :], a, b, ALU.mult).then_inc(split_ready, 1)

            def low(n, s, j):
                dve.wait_ge(hi_ready, n * NS + j + 1)
                nc.vector.tensor_tensor(split_lo[:, j, :], split_prod[:, j % 2, :], split_hi[:, j, :].bitcast(F32),
                                        ALU.subtract).then_inc(lo_ready, 1)

            def small(n, s):
                if s == 0:
                    dve.wait_ge(first_odd_loaded, 16 * SMALL_DMAS)
                turn = (s // 2) % 2
                dve.wait_ge(small_operands_loaded[turn],
                            (n - s % 4) * (8 * SMALL_DMAS) + 16 * SMALL_DMAS * (1 + turn))
                if s >= 1:
                    dve.wait_ge(small_lo_ready, n)
                nc.vector.tensor_tensor(small_prod[:, :], small_operands[:, (s // 2) % 2, 0, :],
                                        small_operands[:, (s // 2) % 2, 1, :], ALU.mult).then_inc(small_ready, 2)

            def small_low(n, s):
                dve.wait_ge(small_hi_ready, n + 1)
                hi, lo = small_halves(s)
                nc.vector.tensor_tensor(small_parts[lo, s % 2, :], small_prod[hi, :],
                                        small_parts[hi, s % 2, :].bitcast(F32), ALU.subtract).then_inc(small_lo_ready, 1)

            def step(n, s):
                dve.wait_ge(operands_loaded[0][s % 2], loads_through(n, s, load_group_dmas(LOAD_GROUPS[0])))
                full(n, s, 0)
                if s == 0:
                    sum_weights()
                dve.wait_ge(operands_loaded[1][s % 2], loads_through(n, s, load_group_dmas(LOAD_GROUPS[1])))
                split(n, s, 0)
                split(n, s, 1)
                if s == 0:
                    split_weights()
                low(n, s, 0)
                dve.wait_ge(operands_loaded[2][s % 2], loads_through(n, s, load_group_dmas(LOAD_GROUPS[2])))
                full(n, s, 1)
                split(n, s, 2)
                low(n, s, 1)
                if s % 2 == 0:
                    small(n, s)
                    low(n, s, 2)
                    small_low(n, s)
                else:
                    small_low(n, s)
                    low(n, s, 2)
                full(n, s, 2)

            step(0, 0)
            step(1, 1)
            with dve.Fori(0, ROUNDS - 1) as q:
                for s in range(2, ROUND + 2):
                    step(q * ROUND + s, s)
            for s in range(2, ROUND):
                step((ROUNDS - 1) * ROUND + s, s)

        @block.scalar
        def _(act):
            act.wait_ge(w_summed, 1)
            nc.scalar.copy(w_hi[:, :, :], w_full[:, SPLIT[0]:SPLIT[0] + NS, :]).then_inc(w_hi_ready, 1)
            act.wait_ge(w_small_summed, 1)
            for at in (0, 2 * QUAD):
                nc.scalar.copy(w_small_parts[at:at + QUAD, :], w_small_sum[:, :]).then_inc(w_small_hi_ready, 1)

            def high(n, s, j):
                act.wait_ge(split_ready, n * NS + j + 1)
                if s >= 1:
                    act.wait_ge(tile_done, tiles_through(n - 1, ("split", j)))
                nc.scalar.copy(split_hi[:, j, :], split_prod[:, j % 2, :]).then_inc(hi_ready, 1)

            def take_h1(n, s):
                act.wait_ge(tile_done, n * TILES)
                if s >= 2:
                    act.wait_ge(h1_transposed, 2 * (n - 1))
                for sub in range(SUBS):
                    nc.scalar.copy(h1[:, sub * BANK:(sub + 1) * BANK], acc[(s - 1) % 2][sub][:, :]).then_inc(h1_ready, 1)

            def spread_x(n, s):
                piece, in_piece = divmod((s - 1) % ROUND, PIECE_STEPS)
                if s == 1:
                    act.wait_ge(diag_ready, 2)
                if in_piece == 0:
                    act.wait_ge(x_turned_loaded[piece], (n - s) * (16 // ROUND) + 16 * ((s - 1) // ROUND + 1))
                if s >= 2:
                    act.wait_ge(gram_done, 2 * (n - 1))
                for parity in range(2):
                    lo = parity * DIM
                    nc.scalar.copy(x_diag[lo:lo + DIM, :, parity * GW:parity * GW + FIELDS],
                                   x_turned[lo:lo + DIM, piece, in_piece * PAIRS_B:(in_piece + 1) * PAIRS_B, :])\
                        .then_inc(x_diag_ready, 1)

            def take_h1_t(n, s, half):
                act.wait_ge(h1_transposed, 2 * n - 1 + half)
                nc.scalar.copy(h1_t[:, half * PER_BANK:(half + 1) * PER_BANK, :],
                               h1_t_ps[:, :].rearrange("p (t j) -> p t j", j=HID)).then_inc(h1_t_ready, 1)

            def take_gram(n, s, half):
                act.wait_ge(gram_done, 2 * n - 1 + half)
                b0 = (s - 1) % ROUND * STEP_B + half * PAIRS_B
                src = gram_ps[half][:, 0:PAIRS_B * GW].rearrange("j (b c) -> j b c", c=GW)[:, :, 0:FIELDS + 1]
                dst = gram[:, :, b0:b0 + PAIRS_B].rearrange("j i b -> j b i")
                nc.scalar.copy(dst, src).then_inc(gram_ready, 1)

            def take_round(q):
                act.wait_ge(round_done, q + 1)
                nc.scalar.copy(out_sb[:, :], out_ps[:, 0:2 * HID]).then_inc(round_copied, 1)
                act.wait_ge(round_copied, q + 1)
                act.dma_start(out[bass.ds(q * P, P), :], out_sb[:, :]).then_inc(out_stored, 16)

            def small_high(n, s):
                act.wait_ge(small_ready, n - s % 2 + 2)
                if s >= 2:
                    act.wait_ge(tile_done, tiles_through(n - 2, ("small", 0)))
                hi, _ = small_halves(s)
                nc.scalar.copy(small_parts[hi, s % 2, :], small_prod[hi, :]).then_inc(small_hi_ready, 1)

            def step(n, s, q=None, lag=True, ahead=True):
                if lag:
                    take_h1(n, s)
                    spread_x(n, s)
                    take_h1_t(n, s, 0)
                if ahead:
                    high(n + 1, s + 1, 0)
                if lag:
                    take_h1_t(n, s, 1)
                if s == ROUND + 1:
                    take_round(q)
                if ahead:
                    high(n + 1, s + 1, 1)
                if lag:
                    take_gram(n, s, 0)
                if ahead:
                    high(n + 1, s + 1, 2)
                if lag:
                    take_gram(n, s, 1)
                if ahead:
                    small_high(n + 1, s + 1)
                if s == ROUND + 1:
                    act.wait_ge(out_stored, q * 16 + 16)

            step(-1, -1, lag=False)
            step(0, 0, lag=False)
            step(1, 1)
            with act.Fori(0, ROUNDS - 1) as q:
                for s in range(2, ROUND + 2):
                    step(q * ROUND + s, s, q)
            for s in range(2, ROUND + 1):
                step((ROUNDS - 1) * ROUND + s, s, ahead=s < ROUND - 1)
            take_round(ROUNDS - 1)
            act.wait_ge(out_stored, ROUNDS * 16)

        @block.tensor
        def _(pe):
            def add(n, s, what, passes):
                first, last = PLACE[what] == 0, PLACE[what] == TILES - 1
                if first and s >= 2:
                    pe.wait_ge(h1_ready, 2 * (n - 1))
                for p, (w, z) in enumerate(passes):
                    for sub in range(SUBS):
                        done = nc.tensor.matmul(acc[s % 2][sub][:, :], w, z[:, sub * BANK:(sub + 1) * BANK],
                                                start=first and p == 0, stop=last and p == len(passes) - 1)
                done.then_inc(tile_done, 1)

            def full(n, s, j):
                pe.wait_ge(full_ready, n * len(FULL) + j + 1)
                add(n, s, ("full", j), [(w_full[:, FULL[j], :], full_prod[:, j, :])])

            def split(n, s, j):
                pe.wait_ge(lo_ready, n * NS + j + 1)
                hi, lo = split_hi[:, j, :], split_lo[:, j, :]
                add(n, s, ("split", j), [(w_hi[:, j, :], hi), (w_hi[:, j, :], lo), (w_lo[:, j, :], hi)])

            def small(n, s):
                pe.wait_ge(small_lo_ready, n + 1)
                add(n, s, ("small", 0), [(w_small_parts[:, :], small_parts[:, s % 2, :])])

            def turn_h1(n, s, half):
                if half == 0:
                    pe.wait_ge(h1_ready, 2 * n)
                if s >= 2 or half:
                    pe.wait_ge(h1_t_ready, 2 * (n - 1) + half)
                for t in range(PER_BANK):
                    c0 = half * BANK + t * P
                    done = nc.tensor.transpose(h1_t_ps[:, t * P:(t + 1) * P], h1[:, c0:c0 + P], ident[:, :])
                done.then_inc(h1_transposed, 1)

            def sum_gram(n, s, half):
                pe.wait_ge(h1_t_ready, 2 * n - 1 + half)
                pe.wait_ge(x_diag_ready, 2 * n)
                if s >= 2:
                    pe.wait_ge(gram_ready, 2 * (n - 1) - 1 + half)
                for t in range(PER_BANK):
                    pair = half * PER_BANK + t
                    done = nc.tensor.matmul(gram_ps[half][:, t * 2 * GW:(t + 1) * 2 * GW], h1_t[:, pair, :],
                                            x_diag[:, pair, :], start=True, stop=True)
                done.then_inc(gram_done, 1)

            def end_round(n):
                pe.wait_ge(w1_loaded, 16 * W1_PARTS)
                pe.wait_ge(gram_ready, 2 * n)
                nc.tensor.transpose(out_ps[:, 0:HID], gram[:, ONES, :], ident[:, :])
                for i in range(FIELDS):
                    done = nc.tensor.matmul(out_ps[:, HID:2 * HID], gram[:, i, :], w1_sb[:, i, :],
                                            start=i == 0, stop=i == FIELDS - 1)
                done.then_inc(round_done, 1)

            def step(n, s):
                lag = s >= 1
                if s == 0:
                    pe.wait_ge(w_summed, 1)
                full(n, s, 0)
                if s == 0:
                    pe.wait_ge(w_lo_ready, 1)
                split(n, s, 0)
                if lag:
                    turn_h1(n, s, 0)
                full(n, s, 1)
                if s == ROUND + 1:
                    end_round(n - 1)
                if lag:
                    turn_h1(n, s, 1)
                split(n, s, 1)
                if s == 0:
                    pe.wait_ge(w_small_lo_ready, 2)
                small(n, s)
                if lag:
                    sum_gram(n, s, 0)
                split(n, s, 2)
                if lag:
                    sum_gram(n, s, 1)
                full(n, s, 2)

            step(0, 0)
            pe.wait_ge(ident_ready, 1)
            step(1, 1)
            with pe.Fori(0, ROUNDS - 1) as q:
                for s in range(2, ROUND + 2):
                    step(q * ROUND + s, s)
                pe.wait_ge(round_copied, q + 1)
            for s in range(2, ROUND):
                step((ROUNDS - 1) * ROUND + s, s)
            for half in range(2):
                turn_h1(STEPS, ROUND, half)
            for half in range(2):
                sum_gram(STEPS, ROUND, half)
            end_round(STEPS)


def kernel(r_x, L0_rec_W0, L0_rec_W1):
    import numpy as _np
    import concourse.bacc as _bacc
    from concourse import mybir as _mybir
    from concourse.bass_utils import run_bass_kernel_spmd as _run

    x, w0, w1 = (_np.asarray(a) for a in (r_x, L0_rec_W0, L0_rec_W1))
    batch, fields, dim = x.shape
    by_field = x.transpose(1, 0, 2).reshape(fields, batch * dim)
    groups, extras, small = (_np.array(pairs) for pairs in pair_places(fields))

    def both_ways(pairs):
        return _np.stack([w0[pairs[..., 0], pairs[..., 1]], w0[pairs[..., 1], pairs[..., 0]]])

    laid_out = (("x_fields", _np.concatenate([by_field, by_field])),
                ("x_small", by_field[small]),
                ("x_dims", x.reshape(batch // 2, 2, fields, dim).transpose(1, 3, 0, 2).reshape(2 * dim, batch // 2, fields)),
                ("w_groups", both_ways(groups)), ("w_extras", both_ways(extras)), ("w_small", both_ways(small)),
                ("w1", w1))

    nc = _bacc.Bacc("TRN2", target_bir_lowering=False, num_devices=1)
    arrays, args = {}, []
    for name, a in laid_out:
        a = _np.ascontiguousarray(a)
        arrays[f"in_{name}"] = a
        args.append(nc.dram_tensor(f"in_{name}", a.shape, _mybir.dt.from_np(a.dtype), kind="ExternalInput").ap())
    out_shape = (batch, w0.shape[2] + w1.shape[2])
    args.append(nc.dram_tensor("out", out_shape, _mybir.dt.float32, kind="ExternalOutput").ap())
    cin_kernel(nc, *args)
    r = _run(nc, [arrays], core_ids=[0])
    return r.results[0]["out"]
```
